# Optimizing a Trainium2 kernel written in Bass

```python
import numpy as np
import jax
import jax.numpy as jnp

def _softmax(x, axis=-1):
    return jax.nn.softmax(x, axis=axis)

def _gelu(x):
    return jax.nn.gelu(x, approximate=True)

def _silu(x):
    return jax.nn.silu(x)

def _sigmoid(x):
    return jax.nn.sigmoid(x)

def _layernorm(x, axis=-1, eps=1e-05):
    m = jnp.mean(x, axis=axis, keepdims=True)
    v = jnp.var(x, axis=axis, keepdims=True)
    return (x - m) / jnp.sqrt(v + eps)

def _scatter_add(tgt, idx, src, axis=0):
    return tgt.at[idx].add(src)

def _segment_sum(src, seg, n):
    return jax.ops.segment_sum(src, seg, n)
kernel_name = 'mk_gnn_preln_d2_gnn_r8_e135e8'

def setup_inputs(seed: int=0):
    np.random.seed(seed)
    _w = jnp.asarray

    def _rec_inputs():
        import jax
        import jax.numpy as jnp
        _gk = jax.random.key(seed)
        x = -0.0001126 + 1 * jax.random.normal(jax.random.fold_in(_gk, 1), (12500, 256), jnp.float32)
        src = jax.random.randint(jax.random.fold_in(_gk, 2), (200000,), 0, 12500, jnp.int32)
        dst = jnp.minimum((12500 * jax.random.uniform(jax.random.fold_in(_gk, 3), (200000,)) ** 2.0).astype(jnp.int32), 99999)
        _o = jnp.argsort(dst, stable=True)
        src = src[_o]
        dst = dst[_o]
        edge_attr_4 = 0.00117183 + 1.0004 * jax.random.normal(jax.random.fold_in(_gk, 12), (200000, 4), jnp.float32)
        edge_attr_8 = -0.000615933 + 0.999959 * jax.random.normal(jax.random.fold_in(_gk, 13), (200000, 8), jnp.float32)
        edge_weight = jax.random.uniform(jax.random.fold_in(_gk, 14), (200000,), jnp.float32, 0.0, 1)
        node_vec1 = jax.random.uniform(jax.random.fold_in(_gk, 15), (12500, 1), jnp.float32, 0.0, 1)
        return (x, src, dst, edge_attr_4, edge_attr_8, edge_weight, node_vec1)
    x, src, dst, edge_attr_4, edge_attr_8, edge_weight, node_vec1 = _rec_inputs()

    def _L0_gnn_setup():
        import jax, jax.numpy as jnp
        import numpy as np
        import math
        N = 3750
        E = 75000
        MUL = 64
        NES = 8
        FCN = 64
        NUM_NEIGHBORS = 20.0
        SILU_NORM = 1.679
        INV_SQRT3 = 1.0 / math.sqrt(3.0)

        def _split(x):
            return (x[:, :MUL], x[:, MUL:].reshape(-1, MUL, 3))
        key = jax.random.key(seed)
        ks = jax.random.split(key, 16)
        inp = {'node_input': jax.random.normal(ks[0], (N, 4 * MUL), jnp.float32), 'node_attr': jnp.ones((N, 1), jnp.float32), 'edge_src': jax.random.randint(ks[1], (E,), 0, N), 'edge_dst': jax.random.randint(ks[2], (E,), 0, N), 'edge_attr': jax.random.normal(ks[3], (E, 4), jnp.float32), 'edge_scalars': jax.random.normal(ks[4], (E, NES), jnp.float32), 'sc_w0': jax.random.normal(ks[5], (MUL, MUL), jnp.float32), 'sc_w1': jax.random.normal(ks[6], (MUL, MUL), jnp.float32), 'lin1_w0': jax.random.normal(ks[7], (MUL, MUL), jnp.float32), 'lin1_w1': jax.random.normal(ks[8], (MUL, MUL), jnp.float32), 'fc_w1': jax.random.normal(ks[9], (NES, FCN), jnp.float32), 'fc_w2': jax.random.normal(ks[10], (FCN, 4 * MUL), jnp.float32), 'lin2_w00': jax.random.normal(ks[11], (MUL, MUL), jnp.float32), 'lin2_w01': jax.random.normal(ks[12], (MUL, MUL), jnp.float32), 'lin2_w10': jax.random.normal(ks[13], (MUL, MUL), jnp.float32), 'lin2_w11': jax.random.normal(ks[14], (MUL, MUL), jnp.float32)}
        return inp
    _L0_gnn_all = _L0_gnn_setup()
    _L0_gnn_in = {k: v for k, v in _L0_gnn_all.items() if k in ('sc_w0', 'sc_w1', 'lin1_w0', 'lin1_w1', 'fc_w1', 'fc_w2', 'lin2_w00', 'lin2_w01', 'lin2_w10', 'lin2_w11')}
    del _L0_gnn_all

    def _L1_gnn_setup():
        import jax, jax.numpy as jnp
        import numpy as np
        N = 12500
        E = 400000
        DI = 256
        DO = 256
        BN_EPS = 1e-05

        def _bn_relu(h, gamma, beta):
            mean = jnp.mean(h, axis=0)
            var = jnp.var(h, axis=0)
            hn = (h - mean) * jax.lax.rsqrt(var + BN_EPS)
            return jax.nn.relu(hn * gamma + beta)
        key = jax.random.key(seed)
        ks = jax.random.split(key, 6)
        x = jax.random.normal(ks[0], (N, DI), dtype=jnp.float32)
        edge_row = jax.random.randint(ks[1], (E,), 0, N, dtype=jnp.int32)
        edge_col = jax.random.randint(ks[2], (E,), 0, N, dtype=jnp.int32)
        edge_vals = jnp.ones((E,), dtype=jnp.float32)
        eps = jnp.zeros((1,), dtype=jnp.float32)
        W1 = jax.random.normal(ks[3], (DI, DO), dtype=jnp.float32) * 0.05
        b1 = jnp.zeros((DO,), dtype=jnp.float32)
        g1 = jnp.ones((DO,), dtype=jnp.float32)
        be1 = jnp.zeros((DO,), dtype=jnp.float32)
        W2 = jax.random.normal(ks[4], (DO, DO), dtype=jnp.float32) * 0.05
        b2 = jnp.zeros((DO,), dtype=jnp.float32)
        g2 = jnp.ones((DO,), dtype=jnp.float32)
        be2 = jnp.zeros((DO,), dtype=jnp.float32)
        return {'x': x, 'edge_row': edge_row, 'edge_col': edge_col, 'edge_vals': edge_vals, 'eps': eps, 'W1': W1, 'b1': b1, 'g1': g1, 'be1': be1, 'W2': W2, 'b2': b2, 'g2': g2, 'be2': be2}
    _L1_gnn_all = _L1_gnn_setup()
    _L1_gnn_in = {k: v for k, v in _L1_gnn_all.items() if k in ('eps', 'W1', 'b1', 'g1', 'be1', 'W2', 'b2', 'g2', 'be2')}
    del _L1_gnn_all
    return {'x': x, 'src': src, 'dst': dst, 'edge_attr_4': edge_attr_4, 'edge_attr_8': edge_attr_8, 'edge_weight': edge_weight, 'node_vec1': node_vec1, 'L0_gnn_sc_w0': _L0_gnn_in['sc_w0'], 'L0_gnn_sc_w1': _L0_gnn_in['sc_w1'], 'L0_gnn_lin1_w0': _L0_gnn_in['lin1_w0'], 'L0_gnn_lin1_w1': _L0_gnn_in['lin1_w1'], 'L0_gnn_fc_w1': _L0_gnn_in['fc_w1'], 'L0_gnn_fc_w2': _L0_gnn_in['fc_w2'], 'L0_gnn_lin2_w00': _L0_gnn_in['lin2_w00'], 'L0_gnn_lin2_w01': _L0_gnn_in['lin2_w01'], 'L0_gnn_lin2_w10': _L0_gnn_in['lin2_w10'], 'L0_gnn_lin2_w11': _L0_gnn_in['lin2_w11'], 'L1_gnn_eps': _L1_gnn_in['eps'], 'L1_gnn_W1': _L1_gnn_in['W1'], 'L1_gnn_b1': _L1_gnn_in['b1'], 'L1_gnn_g1': _L1_gnn_in['g1'], 'L1_gnn_be1': _L1_gnn_in['be1'], 'L1_gnn_W2': _L1_gnn_in['W2'], 'L1_gnn_b2': _L1_gnn_in['b2'], 'L1_gnn_g2': _L1_gnn_in['g2'], 'L1_gnn_be2': _L1_gnn_in['be2']}

def reference(x, src, dst, edge_attr_4, edge_attr_8, edge_weight, node_vec1, L0_gnn_sc_w0, L0_gnn_sc_w1, L0_gnn_lin1_w0, L0_gnn_lin1_w1, L0_gnn_fc_w1, L0_gnn_fc_w2, L0_gnn_lin2_w00, L0_gnn_lin2_w01, L0_gnn_lin2_w10, L0_gnn_lin2_w11, L1_gnn_eps, L1_gnn_W1, L1_gnn_b1, L1_gnn_g1, L1_gnn_be1, L1_gnn_W2, L1_gnn_b2, L1_gnn_g2, L1_gnn_be2):
    import jax
    import jax.numpy as jnp

    def _L0_gnn_ref(node_input, node_attr, edge_src, edge_dst, edge_attr, edge_scalars, sc_w0, sc_w1, lin1_w0, lin1_w1, fc_w1, fc_w2, lin2_w00, lin2_w01, lin2_w10, lin2_w11):
        import jax, jax.numpy as jnp
        import numpy as np
        import math
        N = 3750
        E = 75000
        MUL = 64
        NES = 8
        FCN = 64
        NUM_NEIGHBORS = 20.0
        SILU_NORM = 1.679
        INV_SQRT3 = 1.0 / math.sqrt(3.0)

        def _split(x):
            return (x[:, :MUL], x[:, MUL:].reshape(-1, MUL, 3))
        n = node_input.shape[0]
        inv_mul = 1.0 / math.sqrt(MUL)
        x0, x1 = _split(node_input)
        a = node_attr
        s0 = x0 @ sc_w0 * a * inv_mul
        s1 = jnp.einsum('nuc,uv->nvc', x1, sc_w1) * a[:, :, None] * inv_mul
        y0 = x0 @ lin1_w0 * a * inv_mul
        y1 = jnp.einsum('nuc,uv->nvc', x1, lin1_w1) * a[:, :, None] * inv_mul
        h = jax.nn.silu(edge_scalars @ fc_w1 * (1.0 / math.sqrt(NES))) * SILU_NORM
        w = h @ fc_w2 * (1.0 / math.sqrt(FCN))
        w_a, w_b, w_c, w_d = (w[:, :MUL], w[:, MUL:2 * MUL], w[:, 2 * MUL:3 * MUL], w[:, 3 * MUL:])
        xg0 = y0[edge_src]
        xg1 = y1[edge_src]
        ea0 = edge_attr[:, :1]
        ea1 = edge_attr[:, 1:4]
        mid0 = w_a * xg0 * ea0
        mid1 = w_b * jnp.einsum('euc,ec->eu', xg1, ea1) * INV_SQRT3
        mid2 = (w_c * xg0)[:, :, None] * ea1[:, None, :]
        mid3 = (w_d * ea0)[:, :, None] * xg1
        mids = jnp.concatenate([mid0, mid1, mid2.reshape(-1, 3 * MUL), mid3.reshape(-1, 3 * MUL)], axis=1)
        agg = jax.ops.segment_sum(mids, edge_dst, num_segments=n)
        agg = agg * (1.0 / math.sqrt(NUM_NEIGHBORS))
        z0a = agg[:, :MUL]
        z0b = agg[:, MUL:2 * MUL]
        z1a = agg[:, 2 * MUL:5 * MUL].reshape(n, MUL, 3)
        z1b = agg[:, 5 * MUL:].reshape(n, MUL, 3)
        inv2 = 1.0 / math.sqrt(2 * MUL)
        o0 = (z0a @ lin2_w00 + z0b @ lin2_w01) * a * inv2
        o1 = (jnp.einsum('nuc,uv->nvc', z1a, lin2_w10) + jnp.einsum('nuc,uv->nvc', z1b, lin2_w11)) * a[:, :, None] * inv2
        c_s = math.sin(math.pi / 8.0)
        c_x = math.cos(math.pi / 8.0)
        out0 = c_s * s0 + c_x * o0
        out1 = c_s * s1 + c_x * o1
        return jnp.concatenate([out0, out1.reshape(n, 3 * MUL)], axis=1)

    def _L1_gnn_ref(x, edge_row, edge_col, edge_vals, eps, W1, b1, g1, be1, W2, b2, g2, be2):
        import jax, jax.numpy as jnp
        import numpy as np
        N = 12500
        E = 400000
        DI = 256
        DO = 256
        BN_EPS = 1e-05

        def _bn_relu(h, gamma, beta):
            mean = jnp.mean(h, axis=0)
            var = jnp.var(h, axis=0)
            hn = (h - mean) * jax.lax.rsqrt(var + BN_EPS)
            return jax.nn.relu(hn * gamma + beta)
        n = x.shape[0]
        msgs = edge_vals[:, None] * x[edge_col]
        agg = jax.ops.segment_sum(msgs, edge_row, num_segments=n)
        h = (1.0 + eps[0]) * x + agg
        h = _bn_relu(h @ W1 + b1, g1, be1)
        h = _bn_relu(h @ W2 + b2, g2, be2)
        return h
    h = jnp.maximum(_layernorm(x, axis=-1), 0.0)
    x = x + _L0_gnn_ref(h, node_vec1, src, dst, edge_attr_4, edge_attr_8, L0_gnn_sc_w0, L0_gnn_sc_w1, L0_gnn_lin1_w0, L0_gnn_lin1_w1, L0_gnn_fc_w1, L0_gnn_fc_w2, L0_gnn_lin2_w00, L0_gnn_lin2_w01, L0_gnn_lin2_w10, L0_gnn_lin2_w11)
    h = jnp.maximum(_layernorm(x, axis=-1), 0.0)
    x = x + _L1_gnn_ref(h, src, dst, edge_weight, L1_gnn_eps, L1_gnn_W1, L1_gnn_b1, L1_gnn_g1, L1_gnn_be1, L1_gnn_W2, L1_gnn_b2, L1_gnn_g2, L1_gnn_be2)
    return x

_drawn_inputs = setup_inputs


def setup_inputs(seed=0):
    import zlib

    import numpy as np

    out = dict(_drawn_inputs(seed))
    spreads = {'L1_gnn_b1': (0.0, 0.1),
     'L1_gnn_g1': (1.0, 0.2),
     'L1_gnn_be1': (0.0, 0.1),
     'L1_gnn_b2': (0.0, 0.1),
     'L1_gnn_g2': (1.0, 0.2),
     'L1_gnn_be2': (0.0, 0.1)}
    factors = {}
    for name, (base, spread) in spreads.items():
        noise = np.random.default_rng([zlib.crc32(name.encode()), seed]).standard_normal(out[name].shape)
        drawn = base * np.exp(spread * noise) if base else spread * noise
        out[name] = jnp.asarray(drawn.astype(out[name].dtype))
    for name, factor in factors.items():
        out[name] = (out[name] * factor).astype(out[name].dtype)
    return out
```

```python
import concourse.bass as bass
from concourse import mybir
from contextlib import ExitStack
import math

fp32 = mybir.dt.float32
i32 = mybir.dt.int32
ALU = mybir.AluOpType
ACT = mybir.ActivationFunctionType
AX_X = mybir.AxisListType.X

P = 128
N, E, D, U = 12500, 200000, 256, 64
NES, FCN = 8, 64
NB = -(-N // P)
LAST = N - (NB - 1) * P
T = 2 * -(-E // (2 * P))
TC = -(-T // P)
SENT = NB * P
R = 4
LN_EPS = 1e-5
BN_EPS = 1e-5
CH = 500
NCH = N // CH
ACC_ROWS = NB * 130
BASE, OFF, BODIES = 0, 128, 127


def build_program(nc, x, src_pt, src_row, dst_pt, dst_tp, ea4_pt, ea8_tk, ew_pt, a_pt, sc_w0, sc_w1, lin1_w0, lin1_w1,
                  fc_w1, fc_w2, w00, w01, w10, w11, eps, W1, b1, g1, be1, W2, b2, g2, be2, out):
    ctx = ExitStack()
    with ctx:
        def sb(name, shape, dt=fp32):
            return ctx.enter_context(nc.sbuf_tensor(name, shape, dt))

        def sem(name):
            return ctx.enter_context(nc.semaphore(name))

        y_tab = nc.dram_tensor("y_tab", [N, D], fp32).ap()
        acc = [nc.dram_tensor(f"acc{n}", [ACC_ROWS, D], fp32).ap() for n in range(4)]
        u1_tab = nc.dram_tensor("u1_tab", [P, 2, N], fp32).ap()
        u2_tab = nc.dram_tensor("u2_tab", [P, 2, N], fp32).ap()

        x_all = sb("x_all", [P, NB, D])
        stats = sb("stats", [P, NB, 6])
        mv = sb("mv", [P, NB, 2])
        rstd = sb("rstd", [P, NB])
        nmr = sb("nmr", [P, NB])
        ident = sb("ident", [P, P])
        a_all = sb("a_all", [P, NB])
        blk_tab = sb("blk_tab", [1, 256], i32)
        iota_n = sb("iota_n", [P, P])
        iota_b = sb("iota_b", [P, P])
        ln_eps = sb("ln_eps", [P, 1])
        zero_l = sb("zero_l", [P, P], mybir.dt.bfloat16)
        zero_r = sb("zero_r", [P, 512], mybir.dt.bfloat16)
        dst_f = sb("dst_f", [P, T])
        ea4 = sb("ea4", [P, T, 4])
        ew = sb("ew", [P, T])
        ring = sb("ring", [P, R, 2, D])
        idx = sb("idx", [P, R, 2], i32)

        w_in = sb("w_in", [P, 2, 2, P])
        w_hid = sb("w_hid", [2 * NES, 2 * FCN])
        w_fc2 = sb("w_fc2", [P, 2, D])
        w_out = sb("w_out", [P, 2, U])
        W1s = sb("W1s", [P, 2, D])
        W2s = sb("W2s", [P, 2, D])
        bnp = sb("bnp", [P, 6, 2])
        eps1 = sb("eps1", [P, 1])
        bn_mv = sb("bn_mv", [P, 2, 2, 2])
        bn_s = sb("bn_s", [P, 2, 4, 2])
        st_u = sb("st_u", [P, 2, NB, 6])

        ea8 = sb("ea8", [2 * NES, R, P])
        hT = sb("hT", [P, P])
        M = sb("M", [P, 2, 3, U])
        S = sb("S", [P, 2, 2, U])
        msg = sb("msg", [P, 2, 2, 9, U])
        oh = sb("oh", [P, 2, 2, P])
        zeros = sb("zeros", [P, ACC_ROWS // NB * D // P])
        low = sb("low", [P, P])
        cnt = sb("cnt", [P, 2, 2])
        part_n = sb("part_n", [P, 1])
        work = sb("work", [P, 2, 512])
        work2 = sb("work2", [P, 2, 512])
        tri = sb("tri", [P, P])
        cols = sb("cols", [P, 16])
        trow = sb("trow", [1, 256])
        rows = ea4[:, :, :].rearrange("p t c -> p (t c)")
        iota_t, hit, pick = (rows[:, i * TC * P:(i + 1) * TC * P] for i in range(3))
        dst_t = ring[:, :, :, :].rearrange("p r a d -> p (r a d)")[:, 0:TC * P].rearrange("p (c e) -> p c e", e=P)

        ps = ctx.enter_context(nc.psum_tensor("ps", [P, 8, 512], fp32))

        cols2 = sb("cols2", [P, 2, TC])
        tmp98 = sb("tmp98", [P, 2, NB])
        N_LOADS = 25
        ea_f = ea4[:, :, :].rearrange("p t c -> p (t c)")
        u_sb, r_sb, v_sb = ([ea_f[:, (2 * n + u) * 2 * CH:(2 * n + u + 1) * 2 * CH].rearrange("p (o n) -> p o n", o=2)
                             for u in range(2)] for n in range(3))
        ring_f = ring[:, :, :, :].rearrange("p r a d -> p (r a d)")
        w_sb, r2_sb = ([ring_f[:, (2 * n + u) * D:(2 * n + u + 1) * D].rearrange("p (o n) -> p o n", o=2)
                        for u in range(2)] for n in range(2))
        o_sb = [ring_f[:, (4 + u) * D:(5 + u) * D] for u in range(2)]

        names = """x_ld c_ld e4_ld wt_ld id_ok st_ok sq_ok rs_ok h_ok hT_ps hT_ok y_ps y_ok s_ok
                   rg_ld rg_mm rg_ps rg_ok rg_row tab_ok dve_c setup pool_c act_c
                   pair_ready hid_done silu_done w_done xg_free gc_ok m2_ok p_ok agg_done c1 c2 c3
                   z_ok zT_ps zT_ok o_ps x2_ok zinit
                   st2_ok sq2_ok rs2_ok h2_ok 
                   h2b_ok hh_ok hhT_ps hhT_ok u_ps u1_ok st_done
                   bn_a bn_b bn_c r_ok u2_ps u2_ok st2u r2_ok t_ps o_ok ring_done s_ok0 ib_ok st1_ok zero_st src_ld src_ok srow_ready d_ok cnt_ok u_ok idx_ok c_ps c_ok rows_ps rows_ok rows_free l1_done sum_b""".split()
        s = {n: sem(n) for n in names}
        y_st = [sem(f"y_st{i}") for i in range(2)]
        idx_ld = [sem(f"idx_ld{i}") for i in range(R)]
        gath = [sem(f"gath{i}") for i in range(R)]
        srow_ld = [sem(f"srow_ld{i}") for i in range(R)]
        scat = [sem(f"scat{i}") for i in range(R)]
        acc_ld = [sem(f"acc_ld{i}") for i in range(2)]
        u1_st = [sem(f"u1_st{i}") for i in range(2)]
        u1_ld = [sem(f"u1_ld{i}") for i in range(2)]
        u2_st = [sem(f"u2_st{i}") for i in range(2)]
        u2_ld = [sem(f"u2_ld{i}") for i in range(2)]
        out_st = [sem(f"out_st{i}") for i in range(2)]

        V, A, PE, G, SP = nc.vector, nc.scalar, nc.tensor, nc.gpsimd, nc.sync

        XG = 4
        xcuts = [0, 25, 49, 73, NB - 1]

        def x1_cu(ap):
            return ap.rearrange("p (u c) -> p c u", c=3)

        def blk(eng, b, lo=0, hi=1 << 20):
            first = eng.value_load(blk_tab[0:1, bass.ds(BASE + b, 1)], min_val=0, max_val=1 << 20)
            end = eng.value_load(blk_tab[0:1, bass.ds(BASE + 1 + b, 1)], min_val=1, max_val=1 << 20)
            off = eng.value_load(blk_tab[0:1, bass.ds(OFF + b, 1)], min_val=-(1 << 21), max_val=T)
            return first, end, off

        def end_of_blocks(eng):
            return eng.value_load(blk_tab[0:1, BASE + NB:BASE + NB + 1], min_val=1, max_val=1 << 20)

        def tile0(eng, k, off):
            return eng.snap((k * 2 + off).with_bounds(min_val=0, max_val=T - 2))

        src_f = ea_f[:, 0:T]
        spare = ea_f[:, T:2 * T]
        srow = ring_f[:, 0:R * 2 * P].bitcast(i32)
        rows_f = msg[:, :, :, :, :].rearrange("p s t g u -> p (s t g u)")[:, 0:R * 2 * D]
        rows_sb = rows_f.rearrange("p (r j d) -> p r j d", r=R, j=2)
        Csb = S[:, :, :, :].rearrange("p a b u -> p a (b u)")
        junk = M[:, :, :, :].rearrange("p a b u -> p (a b u)")
        h2blk = work2[:, 0, 0:D]
        acc_sb = [ring_f[:, u * 4 * D:(u + 1) * 4 * D].rearrange("p (a d) -> p a d", a=4) for u in range(2)]

        def msg_slot(eng, k):
            f = msg[:, :, :, :, :].rearrange("p s t g u -> p (s t g u)")
            return f[:, bass.ds((k & 1) * (18 * U), 18 * U)].rearrange("p (t g u) -> p t g u", t=2, g=9)

        def ring_slot(eng, k):
            return ring_f[:, bass.ds((k & (R - 1)) * (2 * D), 2 * D)].rearrange("p (t g u) -> p t g u", t=2, g=4)

        def w_bank(eng, k):
            if isinstance(k, int):
                return bank(1 + (k & 1))
            return bank(1, 2)[:, bass.ds((k & 1) * 512, 512)]

        def z_bank(b):
            return bank(6 + (b & 1)) if isinstance(b, int) else bank(6, 2)[:, bass.ds((b & 1) * 512, 512)]

        def w_slot(eng, k):
            return w_bank(eng, k).rearrange("p (t g u) -> p t g u", t=2, g=4)

        def ea8_slot(eng, k):
            if isinstance(k, int):
                return ea8[:, k & (R - 1), :]
            return ea8[:, :, :].rearrange("p r e -> p (r e)")[:, bass.ds((k & (R - 1)) * P, P)]

        block = ctx.enter_context(nc.Block())


        def bank(i, n=1):
            return ps[:, i:i + n, :].rearrange("p b c -> p (b c)")

        def row0(b, n=P):
            return slice(b * P, b * P + n) if isinstance(b, int) else bass.ds(b * P, n)

        def one(b):
            return slice(b, b + 1) if isinstance(b, int) else bass.ds(b, 1)

        def blocks(eng, body):
            body([(u, u, P, 0) for u in range(2)])
            with eng.Fori(1, NB // 2 - 1) as i:
                body([(i * 2 + u, u, P, i) for u in range(2)])
            body([(NB - 2, 0, P, NB // 2 - 1), (NB - 1, 1, LAST, NB // 2 - 1)])

        def later(i):
            return not (isinstance(i, int) and i == 0)

        def chunks(eng, body):
            body([(u, u, 0) for u in range(2)])
            with eng.Fori(1, NCH // 2) as i:
                body([(i * 2 + u, u, i) for u in range(2)])
            body([(NCH - 1, 0, NCH // 2)])

        def cols_of(c, n):
            return slice(c * n, c * n + n) if isinstance(c, int) else bass.ds(c * n, n)

        @block.sync
        def _(sp):
            sp.dma_start(dst_t.bitcast(i32), dst_tp.rearrange("(c p) e -> p c e", p=P)).then_inc(s["rg_ld"], 16)
            for c in range(XG):
                lo, hi = xcuts[c], xcuts[c + 1]
                sp.dma_start(x_all[:, lo:hi, :],
                             x[lo * P:hi * P, :].rearrange("(b p) d -> p b d", p=P)).then_inc(s["x_ld"], 16)
            sp.wait_ge(s["id_ok"], 1)
            sp.dma_start(x_all[0:LAST, NB - 1, :], x[(NB - 1) * P:N, :]).then_inc(s["x_ld"], 16)
            sp.dma_start(dst_f[:, :].bitcast(i32), dst_pt).then_inc(s["c_ld"], 16)
            sp.dma_start(a_all[:, :], a_pt).then_inc(s["c_ld"], 16)
            sp.dma_start(ew[:, :], ew_pt).then_inc(s["c_ld"], 16)
            sp.wait_ge(s["rg_row"], 2)
            sp.dma_start(ea4[:, :, :], ea4_pt).then_inc(s["e4_ld"], 16)

            def store_y(items):
                for b, u, n, i in items:
                    sp.wait_ge(s["y_ok"], b + 1)
                    sp.dma_start(y_tab[row0(b, n), :], work2[0:n, u, 0:D]).then_inc(y_st[u], 16)
            blocks(sp, store_y)

            sp.wait_ge(s["tab_ok"], 1)
            with sp.Fori(0, NB + 1) as b:
                first, end, off = blk(sp, b)
                with sp.Fori(first, end) as k:
                    t = tile0(sp, k, off)
                    sp.wait_ge(s["pair_ready"], k + 1)
                    sp.nop(nofuse=True)
                    sp.wait_ge(s["hid_done"], k + 1)
                    sp.nop(nofuse=True)
                    for r in range(R):
                        with sp.If(k % R == r):
                            sp.dma_start(idx[:, r, :], src_pt[:, bass.ds(t, 2)]).then_inc(idx_ld[r], 16)
                            sp.dma_start(ea8[:, r, :], ea8_tk[bass.ds(t * NES, 2 * NES), :]).then_inc(idx_ld[r], 16)

            sp.wait_ge(s["st2_ok"], 1)
            sp.dma_start(src_f.bitcast(i32), src_pt).then_inc(s["src_ld"], 16)

            sp.wait_ge(s["ring_done"], 1)

            def load_srow(r, t):
                sp.dma_start(srow[:, r * 2 * P:(r + 1) * 2 * P],
                             src_row[:, bass.ds(t * P, 2 * P) if not isinstance(t, int) else slice(t * P, (t + 2) * P)]
                             .to_broadcast([P, 2 * P])).then_inc(srow_ld[r], 16)
            with sp.Fori(0, NB + 1) as b:
                first, end, off = blk(sp, b)
                with sp.Fori(first, end) as k:
                    t = tile0(sp, k, off)
                    sp.wait_ge(s["d_ok"], k + 1)
                    sp.nop(nofuse=True)
                    for r in range(R):
                        with sp.If(k % R == r):
                            load_srow(r, t)
            total = sp.value_load(blk_tab[0:1, BASE + NB + 1:BASE + NB + 2], min_val=R, max_val=1 << 20)
            sp.wait_ge(s["d_ok"], total + (R - 2))
            sp.nop(nofuse=True)
            for r in range(2):
                load_srow(r, 0)

            sp.wait_ge(s["l1_done"], 1)

            def load_acc(items):
                for b, u, n, i in items:
                    sp.wait_ge(s["hh_ok"], b + 1)
                    sp.nop(nofuse=True)
                    for m in range(4):
                        sp.dma_start(acc_sb[u][:, m, :], acc[m][row0(b, P), :]).then_inc(acc_ld[u], 16)
            blocks(sp, load_acc)

            for u in range(2):
                sp.wait_ge(u1_st[u], 16 * (NB // 2))
            def load_u1(items):
                for c, u, i in items:
                    sp.wait_ge(s["r_ok"], c + 1)
                    sp.nop(nofuse=True)
                    sp.dma_start(u_sb[u], u1_tab[:, :, cols_of(c, CH)]).then_inc(u1_ld[u], 16)
            chunks(sp, load_u1)
            sp.wait_ge(u2_st[0], 16 * (NCH - NCH // 2))
            sp.wait_ge(u2_st[1], 16 * (NCH // 2))
            def load_u2(items):
                for b, u, n, i in items:
                    sp.wait_ge(s["r2_ok"], b + 1)
                    sp.nop(nofuse=True)
                    sp.dma_start(w_sb[u][:, :, 0:n], u2_tab[:, :, row0(b, n)]).then_inc(u2_ld[u], 16)
            blocks(sp, load_u2)

        @block.gpsimd
        def _(g):
            G.memset(x_all[:, NB - 1, :], 0.0).then_inc(s["id_ok"], 1)
            for m in (w_in[:, :, :, :], w_hid[:, :], w_fc2[:, :, :]):
                G.memset(m, 0.0).then_inc(s["wt_ld"], 1)
            G.memset(zero_l[:, :], 0.0).then_inc(s["pool_c"], 1)
            G.memset(zero_r[:, :], 0.0).then_inc(s["pool_c"], 1)
            G.memset(ln_eps[:, :], LN_EPS).then_inc(s["pool_c"], 1)
            G.memset(ident[:, :], 0.0).then_inc(s["pool_c"], 1)
            G.memset(tri[:, :], 0.0).then_inc(s["pool_c"], 1)
            G.iota(iota_t, pattern=[[1, TC * P]], base=0, channel_multiplier=0,
                   allow_small_or_imprecise_dtypes=True).then_inc(s["pool_c"], 1)
            G.iota(iota_n[:, :], pattern=[[1, P]], base=0, channel_multiplier=0,
                   allow_small_or_imprecise_dtypes=True).then_inc(s["pool_c"], 1)
            G.iota(cols[:, 0:1], pattern=[[0, 1]], base=0, channel_multiplier=P,
                   allow_small_or_imprecise_dtypes=True).then_inc(s["pool_c"], 1)
            G.iota(part_n[:, :], pattern=[[0, 1]], base=N, channel_multiplier=1,
                   allow_small_or_imprecise_dtypes=True).then_inc(s["pool_c"], 1)
            G.memset(zeros[:, :], 0.0).then_inc(s["pool_c"], 1)
            g.wait_ge(s["pool_c"], 10)
            G.affine_select(out=ident[:, :], in_=ident[:, :], compare_op=ALU.not_equal, fill=1.0, base=0,
                            pattern=[[-1, P]], channel_multiplier=1).then_inc(s["pool_c"], 1)
            G.affine_select(out=tri[:, :], in_=tri[:, :], compare_op=ALU.is_ge, fill=1.0, base=0,
                            pattern=[[-1, P]], channel_multiplier=1).then_inc(s["pool_c"], 1)

            g.wait_ge(s["tab_ok"], 1)
            for u in range(2):
                g.wait_ge(y_st[u], 16 * (NB // 2))
            g.sem_inc(s["pair_ready"], R)
            bodies = g.value_load(blk_tab[0:1, BODIES:BODIES + 1], min_val=3, max_val=1 << 20)

            def gather_turn(i):
                for r in range(R):
                    g.wait_ge(idx_ld[r], (i + 1) * 32)
                    g.nop(nofuse=True)
                    g.wait_ge(s["xg_free"], i * R + (r + 1))
                    g.nop(nofuse=True)
                    for j in range(2):
                        g.indirect_dma_start(ring[:, r, j, :], None, y_tab,
                                             bass.IndirectOffsetOnAxis(ap=idx[:, r, j:j + 1], axis=0)
                                             ).then_inc(gath[r], 16)
                    if r >= 2 or later(i):
                        g.wait_ge(gath[(r + 2) % R], (i + 1 if r >= 2 else i) * 32)
                        g.nop(nofuse=True)
                        g.sem_inc(s["pair_ready"], 1)
            gather_turn(0)
            with g.Fori(1, bodies) as i:
                gather_turn(i)
            for r in range(2, R):
                g.wait_ge(gath[r], bodies * 32)
                g.nop(nofuse=True)

            g.sem_inc(s["ring_done"], 1)

            g.wait_ge(s["zero_st"], 16 * 4 * NB)
            g.sem_inc(s["rows_free"], R)
            for r in range(2):
                g.wait_ge(srow_ld[r], 16)
                g.sem_inc(s["srow_ready"], 1)

            def scatter_turn(i):
                for r in range(R):
                    g.wait_ge(srow_ld[(r + 2) % R], (i + 1 if r < 2 else i + 2) * 16)
                    g.nop(nofuse=True)
                    g.sem_inc(s["srow_ready"], 1)
                    g.wait_ge(s["idx_ok"], i * R + (r + 1))
                    g.nop(nofuse=True)
                    g.wait_ge(s["rows_ok"], i * R + (r + 2))
                    g.nop(nofuse=True)
                    if r >= 2 or later(i):
                        g.wait_ge(scat[(r + 2) % R], (i + 1 if r >= 2 else i) * 32)
                        g.nop(nofuse=True)
                        g.sem_inc(s["rows_free"], 1)
                    for j in range(2):
                        g.indirect_dma_start(acc[2 * (r % 2) + j],
                                             bass.IndirectOffsetOnAxis(ap=idx[:, r, j:j + 1], axis=0),
                                             rows_sb[:, r, j, :], None, compute_op=ALU.add).then_inc(scat[r], 16)
            scatter_turn(0)
            with g.Fori(1, bodies) as i:
                scatter_turn(i)
            for r in range(2, R):
                g.wait_ge(scat[r], bodies * 32)
                g.nop(nofuse=True)
            g.sem_inc(s["l1_done"], 1)

            def store_u1(items):
                for b, u, n, i in items:
                    g.wait_ge(s["u1_ok"], b + 1)
                    g.nop(nofuse=True)
                    g.dma_start(u1_tab[:, :, row0(b, n)],
                                work2[:, u, D:2 * D].rearrange("p (o n) -> p o n", o=2)[:, :, 0:n]).then_inc(u1_st[u], 16)
            blocks(g, store_u1)

            def store_u2(items):
                for c, u, i in items:
                    g.wait_ge(s["u2_ok"], c + 1)
                    g.nop(nofuse=True)
                    g.dma_start(u2_tab[:, :, cols_of(c, CH)], v_sb[u]).then_inc(u2_st[u], 16)
            chunks(g, store_u2)

            def store_out(items):
                for b, u, n, i in items:
                    g.wait_ge(s["o_ok"], b + 3)
                    g.nop(nofuse=True)
                    g.dma_start(out[row0(b, n), :], o_sb[u][0:n, :]).then_inc(out_st[u], 16)
            blocks(g, store_out)
            for u in range(2):
                g.wait_ge(out_st[u], 16 * (NB // 2))

        @block.scalar
        def _(act):
            act.wait_ge(s["wt_ld"], 3)
            act.nop(nofuse=True)
            h = U
            loads = [(w_in[0:h, 0, 0, 0:h], lin1_w0), (w_in[h:P, 0, 0, h:P], lin1_w1),
                     (w_in[0:h, 1, 0, 0:h], lin1_w1), (w_in[h:P, 1, 0, h:P], lin1_w1),
                     (w_in[0:h, 0, 1, 0:h], sc_w0), (w_in[h:P, 0, 1, h:P], sc_w1),
                     (w_in[0:h, 1, 1, 0:h], sc_w1), (w_in[h:P, 1, 1, h:P], sc_w1),
                     (w_hid[0:NES, 0:FCN], fc_w1), (w_hid[NES:2 * NES, FCN:2 * FCN], fc_w1),
                     (w_fc2[0:FCN, 0, :], fc_w2), (w_fc2[FCN:P, 1, :], fc_w2),
                     (w_out[0:h, 0, :], w00), (w_out[h:P, 0, :], w01),
                     (w_out[0:h, 1, :], w11), (w_out[h:P, 1, :], w10),
                     (W1s[:, :, :], W1.rearrange("(h p) o -> p h o", p=P)),
                     (W2s[:, :, :], W2.rearrange("(h p) o -> p h o", p=P)),
                     (eps1[:, :], eps)]
            loads += [(bnp[:, n, :], v) for n, v in enumerate((b1, g1, be1, b2, g2, be2))]
            for dst, src in loads:
                act.dma_start(dst, src).then_inc(s["setup"], 16)
            act.wait_ge(s["setup"], 16 * len(loads))
            act.nop(nofuse=True)
            c_s, c_x = math.sin(math.pi / 8), math.cos(math.pi / 8)
            A.mul(w_in[:, :, 0, :], w_in[:, :, 0, :], 1 / math.sqrt(U)).then_inc(s["act_c"], 1)
            A.mul(w_in[:, :, 1, :], w_in[:, :, 1, :], c_s / math.sqrt(U)).then_inc(s["act_c"], 1)
            A.mul(w_fc2[:, :, :], w_fc2[:, :, :], 1.679 / math.sqrt(FCN)).then_inc(s["act_c"], 1)
            f_out = c_x / math.sqrt(2 * U) / math.sqrt(20.0)
            A.mul(w_out[0:U, :, :], w_out[0:U, :, :], f_out).then_inc(s["act_c"], 1)
            A.mul(w_out[U:P, 1, :], w_out[U:P, 1, :], f_out).then_inc(s["act_c"], 1)
            A.mul(w_out[U:P, 0, :], w_out[U:P, 0, :], f_out / math.sqrt(3.0)).then_inc(s["act_c"], 1)
            act.sem_inc(s["z_ok"], 2)

            act.wait_ge(s["st_ok"], 1)
            act.nop(nofuse=True)
            A.activation(rstd[:, :], mv[:, :, 1], ACT.Sqrt, bias=ln_eps[:, :]).then_inc(s["sq_ok"], 1)
            act.wait_ge(s["rs_ok"], 1)
            act.nop(nofuse=True)

            def node_act(items):
                for b, u, n, i in items:
                    act.wait_ge(s["hT_ps"], b + 1)
                    act.nop(nofuse=True)
                    A.activation(work[:, u, 0:U], x_all[:, one(b), 0:U].rearrange("p a d -> p (a d)"), ACT.Relu,
                                 bias=nmr[:, one(b)], scale=rstd[:, one(b)])
                    A.activation(work[:, u, U:D].rearrange("p (c u) -> p c u", c=3),
                                 x1_cu(x_all[:, one(b), U:D].rearrange("p a d -> p (a d)")), ACT.Relu,
                                 bias=nmr[:, one(b)], scale=rstd[:, one(b)]).then_inc(s["h_ok"], 1)
                for b, u, n, i in items:
                    act.wait_ge(s["y_ps"], b + 3)
                    if later(i):
                        act.wait_ge(y_st[u], i * 16)
                    act.nop(nofuse=True)
                    A.activation(work2[:, u, 0:D], bank(2 + u)[:, 0:D], ACT.Copy,
                                 scale=a_all[:, one(b)]).then_inc(s["y_ok"], 1)
            act.wait_ge(s["c_ld"], 48)
            act.nop(nofuse=True)
            blocks(act, node_act)

            def silu(n):
                act.wait_ge(s["hid_done"], n + 1 + R)
                act.nop(nofuse=True)
                if not (isinstance(n, int) and n == 0):
                    act.wait_ge(s["w_done"], n)
                    act.nop(nofuse=True)
                A.activation(hT[:, :], bank(3)[:, 0:P], ACT.Silu,
                             scale=1 / math.sqrt(NES)).then_inc(s["silu_done"], 1)

            def copy_sums(b, end):
                act.wait_ge(s["agg_done"], end * 2 + 4)
                act.nop(nofuse=True)
                act.wait_ge(s["zT_ps"], b + 1)
                act.nop(nofuse=True)
                A.activation(work[:, 0, :].rearrange("p (j h u) -> p h j u", j=4, h=2),
                             z_bank(b).rearrange("p (h j u) -> p h j u", j=4, h=2), ACT.Copy).then_inc(s["z_ok"], 1)
            silu(0)
            silu(1)
            act.wait_ge(s["e4_ld"], 16)
            act.nop(nofuse=True)
            for u in range(2):
                act.wait_ge(y_st[u], 16 * (NB // 2))
                act.nop(nofuse=True)
            with act.Fori(0, NB) as b:
                first, end, off = blk(act, b)
                with act.Fori(first, end) as k:
                    t = tile0(act, k, off)
                    m = msg_slot(act, k)
                    act.wait_ge(s["gc_ok"], k + 1)
                    act.nop(nofuse=True)
                    for j in range(2):
                        for c in range(3):
                            last = A.activation(m[:, j, 5 + c, :], m[:, j, 8, :], ACT.Copy,
                                                scale=ea_f[:, bass.ds(t * 4 + (4 * j + 1 + c), 1)])
                    last.then_inc(s["m2_ok"], 1)
                    silu(k + 2)
                for n in range(4):
                    act.dma_start(acc[n][bass.ds(b * (ACC_ROWS // NB), ACC_ROWS // NB), :]
                                  .rearrange("r d -> (r d)").rearrange("(p c) -> p c", p=P),
                                  zeros[:, :]).then_inc(s["zero_st"], 16)
                with act.If(b >= 1):
                    copy_sums(b - 1, first)
            copy_sums(NB - 1, end_of_blocks(act))

            act.wait_ge(s["st2_ok"], 1)
            act.nop(nofuse=True)
            A.activation(rstd[:, :], mv[:, :, 1], ACT.Sqrt, bias=ln_eps[:, :]).then_inc(s["sq2_ok"], 1)
            act.wait_ge(s["rs2_ok"], 1)
            act.nop(nofuse=True)

            def h2_of(b, dst):
                return A.activation(dst, x_all[:, one(b), :].rearrange("p a d -> p (a d)"), ACT.Relu,
                                    bias=nmr[:, one(b)], scale=rstd[:, one(b)])

            act.sem_inc(s["c_ok"], 1)
            act.sem_inc(s["rows_ok"], 1)

            def rows_act(b, h2_from):
                first, end, off = blk(act, b)
                h2_of(h2_from, h2blk).then_inc(s["h2b_ok"], 1)
                with act.Fori(first, end) as k:
                    act.wait_ge(s["c_ps"], k + 2)
                    act.nop(nofuse=True)
                    A.activation(Csb, bank(1)[:, 0:2 * P].rearrange("p (a b) -> p a b", a=2),
                                 ACT.Copy).then_inc(s["c_ok"], 1)
                    act.wait_ge(s["rows_ps"], k + 1)
                    act.wait_ge(s["rows_free"], k + 1)
                    act.nop(nofuse=True)
                    A.activation(rows_f[:, bass.ds((k & (R - 1)) * (2 * D), 2 * D)], bank(2),
                                 ACT.Copy).then_inc(s["rows_ok"], 1)
            with act.Fori(0, NB) as b:
                rows_act(b, b)
            rows_act(NB, NB - 1)

            def gin_act(items):
                for b, u, n, i in items:
                    act.wait_ge(s["hh_ok"], b + 1)
                    act.nop(nofuse=True)
                    h2_of(b, work[:, u, 0:D]).then_inc(s["h2b_ok"], 1)
                for b, u, n, i in items:
                    act.wait_ge(s["hhT_ps"], b + 1)
                    act.wait_ge(s["u_ps"], b + 1)
                    act.nop(nofuse=True)
                    A.activation(work2[:, u, 0:D], bank(4 + u)[:, 0:D], ACT.Copy).then_inc(s["hhT_ok"], 1)
                for b, u, n, i in items:
                    act.wait_ge(s["u_ps"], b + 3)
                    if later(i):
                        act.wait_ge(u1_st[u], i * 16)
                    act.wait_ge(s["st_done"], b + 1)
                    act.nop(nofuse=True)
                    for o in range(2):
                        last = A.activation(work2[:, u, D + o * P:D + (o + 1) * P], bank(6 + u)[:, o * P:(o + 1) * P],
                                            ACT.Identity, bias=bnp[:, 0, o:o + 1])
                    last.then_inc(s["u1_ok"], 1)
            blocks(act, gin_act)

            for l in range(2):
                act.wait_ge(s["bn_a"], l + 1)
                act.nop(nofuse=True)
                A.activation(bn_s[:, l, 0, :], bn_mv[:, l, :, 1], ACT.Sqrt, bias=ln_eps[:, :]).then_inc(s["bn_b"], 1)
                act.wait_ge(s["bn_c"], l + 1)
                act.nop(nofuse=True)
                if l == 0:
                    def bn1_act(items):
                        for c, u, i in items:
                            act.wait_ge(u1_ld[u], i * 16 + 16)
                            act.wait_ge(s["u2_ps"], c + 1)
                            act.nop(nofuse=True)
                            for o in range(2):
                                last = A.activation(r_sb[u][:, o, :], u_sb[u][:, o, :], ACT.Relu,
                                                    bias=bn_s[:, 0, 3, o:o + 1], scale=bn_s[:, 0, 2, o:o + 1])
                            last.then_inc(s["r_ok"], 1)
                        for c, u, i in items:
                            act.wait_ge(s["u2_ps"], c + 3)
                            if later(i):
                                act.wait_ge(u2_st[u], i * 16)
                            act.wait_ge(s["st2u"], c + 1)
                            act.nop(nofuse=True)
                            for o in range(2):
                                last = A.activation(v_sb[u][:, o, :], bank(2 * u + o)[:, 0:CH], ACT.Identity,
                                                    bias=bnp[:, 3, o:o + 1])
                            last.then_inc(s["u2_ok"], 1)
                    act.sem_inc(s["r_ok"], 2)
                    chunks(act, bn1_act)
                else:
                    act.sem_inc(s["r2_ok"], 2)

                    def bn2_act(items):
                        for b, u, n, i in items:
                            act.wait_ge(u2_ld[u], i * 16 + 16)
                            act.wait_ge(s["t_ps"], b + 1)
                            act.nop(nofuse=True)
                            for o in range(2):
                                last = A.activation(r2_sb[u][:, o, :], w_sb[u][:, o, :], ACT.Relu,
                                                    bias=bn_s[:, 1, 3, o:o + 1], scale=bn_s[:, 1, 2, o:o + 1])
                            last.then_inc(s["r2_ok"], 1)
                    blocks(act, bn2_act)

        @block.vector
        def _(dve):
            count = [0]

            def link(ins):
                count[0] += 1
                ins.then_inc(s["dve_c"], 1)
                dve.wait_ge(s["dve_c"], count[0])

            dve.sem_inc(s["hT_ps"], 2)
            dve.sem_inc(s["y_ps"], 2)
            dve.wait_ge(s["rg_ld"], 16)
            dve.wait_ge(s["pool_c"], 12)
            V.tensor_reduce(cols2[:, 0, :], dst_t.bitcast(i32), AX_X, ALU.min).then_inc(s["rg_mm"], 1)
            V.tensor_reduce(cols2[:, 1, :], dst_t.bitcast(i32), AX_X, ALU.max).then_inc(s["rg_mm"], 1)
            link(V.tensor_scalar(cols[:, 1:2], cols[:, 0:1], float(P), None, ALU.add))
            dve.wait_ge(s["rg_ps"], 1)
            TP = TC * P
            link(V.tensor_scalar(hit, bank(4, 4)[:, 0:TP], cols[:, 0:1], None, ALU.is_ge))
            link(V.scalar_tensor_tensor(out=hit, in0=bank(0, 4)[:, 0:TP], scalar=cols[:, 1:2], in1=hit,
                                        op0=ALU.is_lt, op1=ALU.mult))
            link(V.scalar_tensor_tensor(out=pick, in0=iota_t, scalar=-4096.0, in1=hit, op0=ALU.add, op1=ALU.mult))
            link(V.tensor_reduce(cols[:, 2:3], pick, AX_X, ALU.min))
            link(V.scalar_tensor_tensor(out=pick, in0=iota_t, scalar=1.0, in1=hit, op0=ALU.add, op1=ALU.mult))
            link(V.tensor_reduce(cols[:, 3:4], pick, AX_X, ALU.max))
            V.tensor_copy(iota_b[:, :], iota_n[:, :]).then_inc(s["rg_row"], 2)
            link(V.tensor_scalar(cols[:, 4:5], cols[:, 2:3], 4096.0, float(T - 2), ALU.add, ALU.min))
            link(V.tensor_scalar(cols[:, 5:6], cols[:, 3:4], cols[:, 4:5], 1.0, ALU.subtract, ALU.add))
            link(V.tensor_scalar(cols[:, 6:7], cols[:, 5:6], 0.5, -0.25, ALU.mult, ALU.add))
            RND = float(3 << 22)
            link(V.tensor_scalar(cols[:, 7:8], cols[:, 6:7], RND, None, ALU.add))
            V.tensor_scalar(cols[:, 8:9], cols[:, 7:8], -RND, 1.0, ALU.add, ALU.max).then_inc(s["rg_mm"], 1)
            dve.wait_ge(s["rg_ps"], 2)
            link(V.tensor_copy(trow[0:1, 0:P], bank(0)[0:1, 0:P]))
            link(V.scalar_tensor_tensor(out=trow[0:1, P:2 * P], in0=trow[0:1, 0:P], scalar=-2.0,
                                        in1=bank(1)[0:1, 0:P], op0=ALU.mult, op1=ALU.add))
            c = trow[0:1, BODIES:BODIES + 1]
            link(V.tensor_scalar(c, trow[0:1, NB:NB + 1], 7.0, 0.25, ALU.add, ALU.mult))
            link(V.tensor_scalar(c, c, -0.375, None, ALU.add))
            link(V.tensor_scalar(c, c, RND, None, ALU.add))
            link(V.tensor_scalar(c, c, -RND, None, ALU.add))
            link(V.tensor_scalar(trow[0:1, NB + 1:NB + 2], c, float(R), None, ALU.mult))
            V.tensor_copy(blk_tab[0:1, :], trow[0:1, :]).then_inc(s["tab_ok"], 1)
            dve.wait_ge(s["c_ld"], 48)
            V.tensor_copy(dst_f[:, :], dst_f[:, :].bitcast(i32)).then_inc(s["dve_c"], 1)
            count[0] += 1
            dve.wait_ge(s["setup"], 16 * N_LOADS)
            link(V.tensor_scalar(low[:, :], iota_n[:, :], part_n[:, :], float(N), ALU.subtract, ALU.add))
            link(V.tensor_scalar(low[:, :], low[:, :], 0.0, None, ALU.is_lt))
            link(V.tensor_scalar(eps1[:, :], eps1[:, :], 1.0, None, ALU.add))

            def layernorm_stats(ok, sq_ok, rs_ok):
                st = stats[:, :, :]
                t0 = tmp98[:, 0, :]
                V.tensor_tensor(t0, st[:, :, 1], st[:, :, 4], ALU.subtract).then_inc(s["dve_c"], 1)
                V.tensor_tensor(nmr[:, :], st[:, :, 1], st[:, :, 4], ALU.add).then_inc(s["dve_c"], 1)
                V.tensor_tensor(tmp98[:, 1, :], st[:, :, 2], st[:, :, 5], ALU.add).then_inc(s["dve_c"], 1)
                count[0] += 3
                dve.wait_ge(s["dve_c"], count[0])
                link(V.tensor_tensor(t0, t0, t0, ALU.mult))
                link(V.tensor_scalar(mv[:, :, 0], nmr[:, :], 0.5, None, ALU.mult))
                link(V.tensor_scalar(t0, t0, 0.25, None, ALU.mult))
                V.scalar_tensor_tensor(out=mv[:, :, 1], in0=tmp98[:, 1, :], scalar=1.0 / D, in1=t0,
                                       op0=ALU.mult, op1=ALU.add).then_inc(ok, 1)
                dve.wait_ge(sq_ok, 1)
                link(V.reciprocal(rstd[:, :], rstd[:, :]))
                V.scalar_tensor_tensor(out=nmr[:, :], in0=mv[:, :, 0], scalar=-1.0, in1=rstd[:, :],
                                       op0=ALU.mult, op1=ALU.mult).then_inc(rs_ok, 1)

            dve.wait_ge(s["x_ld"], 16 * (XG + 1))
            with dve.Fori(0, NB) as b:
                V.bn_stats(stats[:, one(b), :].rearrange("p a d -> p (a d)"),
                           x_all[:, one(b), :].rearrange("p a d -> p (a d)")).then_inc(s["s_ok0"], 1)
            dve.wait_ge(s["s_ok0"], NB)
            layernorm_stats(s["st_ok"], s["sq_ok"], s["rs_ok"])
            dve.sem_inc(s["s_ok"], 2)

            def one_hots(t, j):
                V.tensor_scalar(oh[:, j, 0, :], iota_b[:, :], dst_f[:, bass.ds(t + j, 1)],
                                ea_f[:, bass.ds(t * 4 + 4 * j, 1)], ALU.is_equal, ALU.mult)
                V.tensor_scalar(oh[:, j, 1, :], iota_b[:, :], dst_f[:, bass.ds(t + j, 1)], None, ALU.is_equal)

            def node_dve(items):
                for b, u, n, i in items:
                    dve.wait_ge(s["hT_ps"], b + 3)
                    dve.wait_ge(s["y_ps"], b + 1)
                    V.tensor_copy(work[:, u, D:2 * D], bank(u)[:, 0:D]).then_inc(s["hT_ok"], 1)
                for b, u, n, i in items:
                    dve.wait_ge(s["y_ps"], b + 3)
                    add_block(b, bank(4 + u)[:, 0:D], s["s_ok"])

            def add_block(b, o, done):
                xb = x_all[:, one(b), :].rearrange("p a d -> p (a d)")
                V.scalar_tensor_tensor(out=xb[:, 0:U], in0=o[:, 0:U], scalar=a_all[:, one(b)], in1=xb[:, 0:U],
                                       op0=ALU.mult, op1=ALU.add)
                V.scalar_tensor_tensor(out=x1_cu(xb[:, U:D]), in0=o[:, U:D].rearrange("p (c u) -> p c u", c=3),
                                       scalar=a_all[:, one(b)], in1=x1_cu(xb[:, U:D]),
                                       op0=ALU.mult, op1=ALU.add).then_inc(done, 1)
            blocks(dve, node_dve)

            dve.wait_ge(s["e4_ld"], 16)
            dve.sem_inc(s["xg_free"], R)
            dve.sem_inc(s["zT_ok"], 1)
            dve.sem_inc(s["x2_ok"], 3)

            def copy_transposed(b):
                dve.wait_ge(s["zT_ps"], b + 2)
                dve.wait_ge(s["o_ps"], b + 3)
                V.tensor_copy(work[:, 1, :], bank(4)).then_inc(s["zT_ok"], 1)

            def add_sums(b):
                dve.wait_ge(s["o_ps"], b + 4)
                add_block(b, bank(5)[:, 0:D], s["x2_ok"])
                dve.wait_ge(s["x2_ok"], b + 4)
                dve.nop(nofuse=True)
                V.bn_stats(stats[:, one(b), :].rearrange("p a d -> p (a d)"),
                           x_all[:, one(b), :].rearrange("p a d -> p (a d)")).then_inc(s["st1_ok"], 1)
            with dve.Fori(0, NB) as b:
                first, end, off = blk(dve, b)
                with dve.Fori(first, end) as k:
                    t = tile0(dve, k, off)
                    m = msg_slot(dve, k)
                    xg = ring_slot(dve, k)
                    w = w_slot(dve, k)
                    ea = ea_f[:, bass.ds(t * 4, 8)].rearrange("p (t c) -> p t c", t=2)
                    dve.wait_ge(s["pair_ready"], k + (1 + R))
                    dve.wait_ge(s["w_done"], k + 1)
                    dve.wait_ge(s["agg_done"], k * 2 + 2)
                    V.tensor_tensor(m[:, :, 0::8, :], w[:, :, 0::2, :],
                                    xg[:, :, 0:1, :].to_broadcast([P, 2, 2, U]), ALU.mult).then_inc(s["gc_ok"], 1)
                    V.tensor_tensor(M[:, :, :, :], xg[:, :, 1:4, :],
                                    ea[:, :, 1:4].unsqueeze(3).to_broadcast([P, 2, 3, U]), ALU.mult).then_inc(s["c1"], 1)
                    V.tensor_tensor(m[:, :, 1:4, :], xg[:, :, 1:4, :],
                                    w[:, :, 3:4, :].to_broadcast([P, 2, 3, U]), ALU.mult).then_inc(s["xg_free"], 1)
                    dve.wait_ge(s["c1"], k + 1)
                    V.tensor_tensor(S[:, 0, :, :], M[:, :, 0, :], M[:, :, 1, :], ALU.add).then_inc(s["c2"], 1)
                    dve.wait_ge(s["agg_done"], k * 2 + 3)
                    one_hots(t, 0)
                    dve.wait_ge(s["c2"], k + 1)
                    V.tensor_tensor(S[:, 1, :, :], S[:, 0, :, :], M[:, :, 2, :], ALU.add).then_inc(s["c3"], 1)
                    dve.wait_ge(s["agg_done"], k * 2 + 4)
                    one_hots(t, 1)
                    dve.wait_ge(s["c3"], k + 1)
                    V.tensor_tensor(m[:, :, 4, :], w[:, :, 1, :], S[:, 1, :, :], ALU.mult).then_inc(s["p_ok"], 1)
                V.tensor_scalar(iota_b[:, :], iota_b[:, :], float(P), None, ALU.add).then_inc(s["ib_ok"], 1)
                with dve.If(b >= 3):
                    add_sums((b - 3).with_bounds(min_val=0, max_val=NB - 4))
                with dve.If(b >= 2):
                    copy_transposed(b - 2)
                dve.wait_ge(s["ib_ok"], b + 1)
            add_sums(NB - 3)
            copy_transposed(NB - 2)
            add_sums(NB - 2)
            copy_transposed(NB - 1)
            add_sums(NB - 1)
            dve.wait_ge(s["st1_ok"], NB)
            dve.sem_inc(s["xg_free"], R)
            layernorm_stats(s["st2_ok"], s["sq2_ok"], s["rs2_ok"])

            V.tensor_copy(iota_b[:, :], iota_n[:, :]).then_inc(s["ib_ok"], 1)
            dve.wait_ge(s["ib_ok"], NB + 1)
            dve.sem_inc(s["d_ok"], R)
            dve.wait_ge(s["src_ld"], 16)
            V.tensor_copy(src_f, src_f.bitcast(i32)).then_inc(s["src_ok"], 1)
            dve.wait_ge(s["src_ok"], 1)
            V.tensor_scalar(spare, src_f, -1.0, part_n[:, :], ALU.mult, ALU.add).then_inc(s["src_ok"], 1)
            dve.wait_ge(s["src_ok"], 2)

            with dve.Fori(0, NB + 1) as b:
                first, end, off = blk(dve, b)
                with dve.Fori(first, end) as k:
                    t = tile0(dve, k, off)
                    sr = srow[:, bass.ds((k & (R - 1)) * (2 * P), 2 * P)]
                    dve.wait_ge(s["srow_ready"], k + 1)
                    for j in range(2):
                        last = V.scalar_tensor_tensor(out=junk[:, j * P:(j + 1) * P], in0=sr[:, j * P:(j + 1) * P],
                                                      scalar=src_f[:, bass.ds(t + j, 1)], in1=low[:, :],
                                                      op0=ALU.is_equal, op1=ALU.mult,
                                                      accum_out=cnt[:, 0, j:j + 1])
                    last.then_inc(s["cnt_ok"], 1)
                    dve.wait_ge(s["c_ps"], k + 1)
                    for j in range(2):
                        V.tensor_scalar(oh[:, j, 0, :], iota_b[:, :], dst_f[:, bass.ds(t + j, 1)], None, ALU.is_equal)
                        last = V.tensor_scalar(oh[:, j, 1, :], sr[:, j * P:(j + 1) * P], src_f[:, bass.ds(t + j, 1)],
                                               ew[:, bass.ds(t + j, 1)], ALU.is_equal, ALU.mult)
                    last.then_inc(s["d_ok"], 1)
                    dve.wait_ge(s["cnt_ok"], k + 1)
                    V.scalar_tensor_tensor(out=cnt[:, 1, :], in0=cnt[:, 0, :], scalar=0.0, in1=spare[:, bass.ds(t, 2)],
                                           op0=ALU.is_gt, op1=ALU.mult).then_inc(s["u_ok"], 1)
                    dve.wait_ge(s["u_ok"], k + 1)
                    dve.wait_ge(s["rows_free"], k + 1)
                    V.tensor_tensor(idx[:, :, :].rearrange("p r j -> p (r j)")[:, bass.ds((k & (R - 1)) * 2, 2)],
                                    cnt[:, 1, :], src_f[:, bass.ds(t, 2)], ALU.add).then_inc(s["idx_ok"], 1)
                dve.wait_ge(s["d_ok"], end + R)
                V.tensor_scalar(iota_b[:, :], iota_b[:, :], float(P), None, ALU.add).then_inc(s["ib_ok"], 1)
                dve.wait_ge(s["ib_ok"], b + (NB + 2))

            dve.sem_inc(s["hh_ok"], 2)
            dve.sem_inc(s["st_done"], 2)

            def gin_dve(items):
                for b, u, n, i in items:
                    dve.wait_ge(acc_ld[u], i * 64 + 64)
                    V.tensor_tensor(acc_sb[u][:, 0:2, :], acc_sb[u][:, 0:2, :], acc_sb[u][:, 2:4, :],
                                    ALU.add).then_inc(s["sum_b"], 1)
                for b, u, n, i in items:
                    dve.wait_ge(s["sum_b"], i * 4 + 2)
                    dve.wait_ge(s["h2b_ok"], b + (NB + 2))
                    if later(i):
                        dve.wait_ge(s["hhT_ps"], b - 1)
                    V.scalar_tensor_tensor(out=work[:, u, D:2 * D], in0=work[:, u, 0:D], scalar=eps1[:, :],
                                           in1=acc_sb[u][:, 0, :], op0=ALU.mult, op1=ALU.add).then_inc(s["sum_b"], 1)
                for b, u, n, i in items:
                    dve.wait_ge(s["sum_b"], i * 4 + 4)
                    V.tensor_tensor(work[:, u, D:2 * D], work[:, u, D:2 * D], acc_sb[u][:, 1, :],
                                    ALU.add).then_inc(s["hh_ok"], 1)
                for b, u, n, i in items:
                    dve.wait_ge(s["u1_ok"], b + 1)
                    dve.nop(nofuse=True)
                    for o in range(2):
                        last = V.bn_stats(st_u[:, o, one(b), :].rearrange("p a d -> p (a d)"),
                                          work2[:, u, D + o * P:D + o * P + n])
                    last.then_inc(s["st_done"], 1)
            blocks(dve, gin_dve)

            def batchnorm_params(l, groups):
                for o in range(2):
                    last = V.bn_aggr(bn_mv[:, l, o, :], st_u[:, o, 0:groups, :].rearrange("p b s -> p (b s)"))
                last.then_inc(s["bn_a"], 1)
                dve.wait_ge(s["bn_b"], l + 1)
                link(V.reciprocal(bn_s[:, l, 1, :], bn_s[:, l, 0, :]))
                link(V.tensor_tensor(bn_s[:, l, 2, :], bn_s[:, l, 1, :], bnp[:, 3 * l + 1, :], ALU.mult))
                link(V.tensor_tensor(bn_s[:, l, 3, :], bn_mv[:, l, :, 0], bn_s[:, l, 2, :], ALU.mult))
                V.tensor_tensor(bn_s[:, l, 3, :], bnp[:, 3 * l + 2, :], bn_s[:, l, 3, :], ALU.subtract).then_inc(s["bn_c"], 1)

            dve.wait_ge(s["st_done"], NB + 2)
            batchnorm_params(0, NB)
            dve.wait_ge(s["bn_c"], 1)
            dve.sem_inc(s["st2u"], 2)
            dve.sem_inc(s["u2_ps"], 2)

            def bn1_dve(items):
                for c, u, i in items:
                    dve.wait_ge(s["u2_ok"], c + 1)
                    dve.nop(nofuse=True)
                    for o in range(2):
                        last = V.bn_stats(st_u[:, o, one(c), :].rearrange("p a d -> p (a d)"), v_sb[u][:, o, :])
                    last.then_inc(s["st2u"], 1)
            chunks(dve, bn1_dve)
            dve.wait_ge(s["st2u"], NCH + 2)
            batchnorm_params(1, NCH)
            dve.sem_inc(s["t_ps"], 2)

            def bn2_dve(items):
                for b, u, n, i in items:
                    dve.wait_ge(s["t_ps"], b + 3)
                    if later(i):
                        dve.wait_ge(out_st[u], i * 16)
                    V.tensor_tensor(o_sb[u][:, :], bank(4 + u)[:, 0:D],
                                    x_all[:, one(b), :].rearrange("p a d -> p (a d)"), ALU.add).then_inc(s["o_ok"], 1)
            blocks(dve, bn2_dve)

        @block.tensor
        def _(pe):
            pe.wait_ge(s["pool_c"], 12)
            pe.wait_ge(s["rg_mm"], 2)
            for m in range(2):
                for c in range(TC):
                    last = PE.matmul(bank(4 * m, 4)[:, c * P:(c + 1) * P],
                                     cols2[:, m, c:c + 1].to_broadcast([P, P]), ident[:, :], start=True, stop=True)
            last.then_inc(s["rg_ps"], 1)
            pe.wait_ge(s["rg_mm"], 3)
            PE.matmul(bank(0)[0:1, 0:P], cols[0:NB, 8:9], tri[0:NB, :], start=True, stop=True)
            PE.matmul(bank(1)[0:1, 0:P], cols[0:NB, 4:5], ident[0:NB, :], start=True, stop=True).then_inc(s["rg_ps"], 1)
            pe.wait_ge(s["tab_ok"], 1)
            pe.wait_ge(s["act_c"], 6)

            def node_pe(items):
                for b, u, n, i in items:
                    pe.wait_ge(s["h_ok"], b + 1)
                    pe.wait_ge(s["s_ok"], b + 1)
                    for o in range(2):
                        last = PE.transpose(bank(u)[:, o * P:(o + 1) * P], work[:, u, o * P:(o + 1) * P], ident[:, :])
                    last.then_inc(s["hT_ps"], 1)
                for b, u, n, i in items:
                    pe.wait_ge(s["hT_ok"], b + 1)
                    for o in range(2):
                        for m in range(2):
                            last = PE.matmul(bank(2 + 2 * m + u)[:, o * P:(o + 1) * P],
                                             work[:, u, D + o * P:D + (o + 1) * P],
                                             w_in[:, o, m, :], start=True, stop=True)
                    last.then_inc(s["y_ps"], 1)
            blocks(pe, node_pe)

            pe.wait_ge(s["y_ok"], NB)
            pe.wait_ge(s["s_ok"], NB + 2)
            pe.sem_inc(s["hid_done"], R)
            pe.sem_inc(s["agg_done"], 4)
            pe.sem_inc(s["zT_ps"], 1)
            pe.sem_inc(s["o_ps"], 3)

            def hidden(n):
                pe.wait_ge(s["pair_ready"], n + (1 + R))
                if not isinstance(n, int):
                    pe.wait_ge(s["silu_done"], n)
                elif n:
                    pe.wait_ge(s["silu_done"], n)
                PE.matmul(bank(3)[:, 0:P], w_hid[:, :], ea8_slot(pe, n), start=True, stop=True).then_inc(s["hid_done"], 1)

            def weights(n):
                pe.wait_ge(s["silu_done"], n + 1)
                PE.matmul(w_bank(pe, n), hT[:, :], w_fc2[:, :, :].rearrange("p a d -> p (a d)"),
                          start=True, stop=True).then_inc(s["w_done"], 1)

            def transpose_sums(b):
                pe.wait_ge(s["z_ok"], b + 3)
                pe.wait_ge(s["zT_ok"], b + 1)
                for j in range(4):
                    last = PE.transpose(bank(4)[:, j * P:(j + 1) * P], work[:, 0, j * P:(j + 1) * P], ident[:, :])
                last.then_inc(s["zT_ps"], 1)

            def lin2(b):
                pe.wait_ge(s["zT_ok"], b + 2)
                pe.wait_ge(s["x2_ok"], b + 3)
                for j in range(4):
                    last = PE.matmul(bank(5)[:, j * U:(j + 1) * U], work[:, 1, j * P:(j + 1) * P],
                                     w_out[:, min(j, 1), :], start=True, stop=True)
                last.then_inc(s["o_ps"], 1)
            hidden(0)
            weights(0)
            hidden(1)
            weights(1)
            with pe.Fori(0, NB) as b:
                first, end, off = blk(pe, b)
                pe.wait_ge(s["z_ok"], b + 1)
                PE.matmul(z_bank(b), zero_l[:, :], zero_r[:, :], start=True, stop=False, skip_group_check=True)
                z = z_bank(b)
                with pe.Fori(first, end) as k:
                    m = msg_slot(pe, k)
                    hidden(k + 2)
                    pe.wait_ge(s["m2_ok"], k + 1)
                    pe.wait_ge(s["p_ok"], k + 1)
                    for j in range(2):
                        for e in range(2):
                            last = PE.matmul(z[:, e * D:(e + 1) * D], oh[:, j, e, :],
                                             m[:, j, 4 * e:4 * e + 4, :].rearrange("p a u -> p (a u)"),
                                             start=False, stop=True, skip_group_check=True)
                        last.then_inc(s["agg_done"], 1)
                    weights(k + 2)
                with pe.If(b >= 2):
                    lin2(b - 2)
                with pe.If(b >= 1):
                    transpose_sums(b - 1)
            lin2(NB - 2)
            transpose_sums(NB - 1)
            lin2(NB - 1)

            pe.wait_ge(s["x2_ok"], NB + 3)
            pe.sem_inc(s["hid_done"], 2)
            pe.sem_inc(s["c_ps"], 1)
            with pe.Fori(0, NB + 1) as b:
                first, end, off = blk(pe, b)
                with pe.Fori(first, end) as k:
                    pe.wait_ge(s["d_ok"], k + (R + 1))
                    pe.wait_ge(s["c_ok"], k + 1)
                    for j in range(2):
                        last = PE.matmul(bank(1)[:, j * P:(j + 1) * P], oh[:, j, 0, :], oh[:, j, 1, :],
                                         start=True, stop=True)
                    last.then_inc(s["c_ps"], 1)
                    pe.wait_ge(s["h2b_ok"], b + 1)
                    pe.wait_ge(s["rows_ok"], k + 1)
                    pe.wait_ge(s["c_ok"], k + 2)
                    for j in range(2):
                        last = PE.matmul(bank(2)[:, j * D:(j + 1) * D], Csb[:, j, :], h2blk, start=True, stop=True)
                    last.then_inc(s["rows_ps"], 1)

            pe.sem_inc(s["u_ps"], 2)

            def gin_pe(items):
                for b, u, n, i in items:
                    pe.wait_ge(s["hh_ok"], b + 3)
                    for o in range(2):
                        last = PE.transpose(bank(4 + u)[:, o * P:(o + 1) * P], work[:, u, D + o * P:D + (o + 1) * P],
                                            ident[:, :])
                    last.then_inc(s["hhT_ps"], 1)
                for b, u, n, i in items:
                    pe.wait_ge(s["hhT_ok"], b + 1)
                    for o in range(2):
                        for kk in range(2):
                            last = PE.matmul(bank(6 + u)[:, o * P:(o + 1) * P], W1s[:, kk, o * P:(o + 1) * P],
                                             work2[:, u, kk * P:(kk + 1) * P], start=(kk == 0), stop=(kk == 1))
                    last.then_inc(s["u_ps"], 1)
            blocks(pe, gin_pe)

            def bn1_pe(items):
                for c, u, i in items:
                    pe.wait_ge(s["r_ok"], c + 3)
                    for o in range(2):
                        for kk in range(2):
                            last = PE.matmul(bank(2 * u + o)[:, 0:CH], W2s[:, kk, o * P:(o + 1) * P],
                                             r_sb[u][:, kk, :], start=(kk == 0), stop=(kk == 1))
                    last.then_inc(s["u2_ps"], 1)
            chunks(pe, bn1_pe)

            def bn2_pe(items):
                for b, u, n, i in items:
                    pe.wait_ge(s["r2_ok"], b + 3)
                    pe.wait_ge(s["o_ok"], b + 1)
                    for o in range(2):
                        last = PE.transpose(bank(4 + u)[:, o * P:(o + 1) * P], r2_sb[u][:, o, :], ident[:, :])
                    last.then_inc(s["t_ps"], 1)
            pe.sem_inc(s["o_ok"], 2)
            blocks(pe, bn2_pe)


def kernel(**inputs):
    import numpy as np
    import concourse.bacc as bacc
    from concourse.bass_utils import run_bass_kernel_spmd

    def edges(a, fill=0):
        a = np.asarray(a)
        p = np.full((T * P,) + a.shape[1:], fill, a.dtype)
        p[:E] = a
        return p.reshape((T, P) + a.shape[1:])

    dst = edges(inputs["dst"], SENT)
    dst_tp = np.full((TC * P, P), SENT, dst.dtype)
    dst_tp[:T] = dst
    a_pad = np.zeros((NB * P,), np.float32)
    a_pad[:N] = np.asarray(inputs["node_vec1"])[:, 0]
    arrays = {
        "x": inputs["x"],
        "src_pt": edges(inputs["src"]).T,
        "src_row": edges(inputs["src"]).reshape(1, T * P),
        "dst_pt": dst.T,
        "dst_tp": dst_tp,
        "ea4_pt": edges(inputs["edge_attr_4"]).transpose(1, 0, 2),
        "ea8_tk": edges(inputs["edge_attr_8"]).transpose(0, 2, 1).reshape(T * NES, P),
        "ew_pt": edges(inputs["edge_weight"]).T,
        "a_pt": a_pad.reshape(NB, P).T,
    }
    for n in ("sc_w0", "sc_w1", "lin1_w0", "lin1_w1", "fc_w1", "fc_w2", "lin2_w00", "lin2_w01", "lin2_w10", "lin2_w11"):
        arrays[n] = inputs["L0_gnn_" + n]
    arrays["eps"] = np.broadcast_to(np.asarray(inputs["L1_gnn_eps"])[None, :], (P, 1))
    for n in ("W1", "b1", "g1", "be1", "W2", "b2", "g2", "be2"):
        a = inputs["L1_gnn_" + n]
        arrays[n] = a if n in ("W1", "W2") else np.asarray(a).reshape(2, P).T

    nc = bacc.Bacc("TRN2", target_bir_lowering=False, num_devices=1)
    feeds, args = {}, []
    for n, a in arrays.items():
        a = np.ascontiguousarray(a)
        feeds[f"in_{n}"] = a
        args.append(nc.dram_tensor(f"in_{n}", a.shape, mybir.dt.from_np(a.dtype), kind="ExternalInput").ap())
    out = nc.dram_tensor("out", (N, D), fp32, kind="ExternalOutput").ap()
    build_program(nc, *args, out)
    r = run_bass_kernel_spmd(nc, [feeds], core_ids=[0])
    return r.results[0]["out"]
```
